# Optimizing a Trainium2 kernel written in Bass

```python
import numpy as np
import jax
import jax.numpy as jnp

def _softmax(x, axis=-1):
    return jax.nn.softmax(x, axis=axis)

def _gelu(x):
    return jax.nn.gelu(x, approximate=True)

def _silu(x):
    return jax.nn.silu(x)

def _sigmoid(x):
    return jax.nn.sigmoid(x)

def _layernorm(x, axis=-1, eps=1e-05):
    m = jnp.mean(x, axis=axis, keepdims=True)
    v = jnp.var(x, axis=axis, keepdims=True)
    return (x - m) / jnp.sqrt(v + eps)

def _scatter_add(tgt, idx, src, axis=0):
    return tgt.at[idx].add(src)

def _segment_sum(src, seg, n):
    return jax.ops.segment_sum(src, seg, n)
kernel_name = 'mk_decoder_postln_d1_seqx_r8_a50914'

def setup_inputs(seed: int=0):
    np.random.seed(seed)
    _w = jnp.asarray

    def _rec_inputs():
        import jax
        import jax.numpy as jnp
        _rk = jax.random.key(seed)
        x = -0.0003929 + 0.9999 * jax.random.normal(jax.random.fold_in(_rk, 1), (32, 128, 128), jnp.float32)
        _lenS = 128 - jax.random.randint(jax.random.fold_in(_rk, 7), (32,), 0, max(1, 128 // 4) + 1, jnp.int32)
        _lenS2 = 128 - jax.random.randint(jax.random.fold_in(_rk, 8), (32,), 0, max(1, 128 // 4) + 1, jnp.int32)
        _ctx_1024P = jax.random.normal(jax.random.fold_in(_rk, 11), (32, 16, 128), jnp.float32)
        _ctx_1024c = jax.random.dirichlet(jax.random.fold_in(_rk, 511), 0.3 * jnp.ones((16,), jnp.float32), (32, 128))
        _ctx_1024t = jnp.einsum('bsk,bkd->bsd', _ctx_1024c, _ctx_1024P)
        _ctx_1024t = _ctx_1024t * jax.lax.rsqrt(jnp.mean(jnp.square(_ctx_1024t)) + 1e-12) * 0.953939
        ctx_1024 = 2.81802e-05 + 1.00001 * (_ctx_1024t + 0.3 * jax.random.normal(jax.random.fold_in(_rk, 611), (32, 128, 128), jnp.float32))
        return (x, ctx_1024)
    x, ctx_1024 = _rec_inputs()

    def _L0_attn_setup():
        import jax, jax.numpy as jnp
        import numpy as np
        import math
        B, S, D = (4, 256, 128)
        H = 16
        HD = D // H
        DL = 32
        LAMBDA_DECAY = 0.01
        key = jax.random.key(seed)
        ks = jax.random.split(key, 8)
        sc = lambda fan_in: 1.0 / math.sqrt(fan_in)
        return {'x': jax.random.normal(ks[0], (B, S, D), dtype=jnp.float32), 'W_q': jax.random.normal(ks[1], (D, D), dtype=jnp.float32) * sc(D), 'W_k': jax.random.normal(ks[2], (D, D), dtype=jnp.float32) * sc(D), 'W_v': jax.random.normal(ks[3], (D, D), dtype=jnp.float32) * sc(D), 'W_o': jax.random.normal(ks[4], (D, D), dtype=jnp.float32) * sc(D), 'W_down_kv': jax.random.normal(ks[5], (D, DL), dtype=jnp.float32) * sc(D), 'W_up_k': jax.random.normal(ks[6], (DL, D), dtype=jnp.float32) * sc(DL), 'W_up_v': jax.random.normal(ks[7], (DL, D), dtype=jnp.float32) * sc(DL)}
    _L0_attn_all = _L0_attn_setup()
    _L0_attn_in = {k: v for k, v in _L0_attn_all.items() if k in ('W_q', 'W_k', 'W_v', 'W_o', 'W_down_kv', 'W_up_k', 'W_up_v')}
    del _L0_attn_all

    def _L0_xattn_setup():
        import jax, jax.numpy as jnp
        import numpy as np
        EMBED_DIM = 128
        NUM_HEADS = 16
        HEAD_DIM = EMBED_DIM // NUM_HEADS
        B, S = (4, 512)

        def _split_heads(x):
            b, s, e = x.shape
            return x.reshape(b, s, NUM_HEADS, HEAD_DIM).transpose(0, 2, 1, 3)
        key = jax.random.key(seed)
        k0, k1, k2, k3, k4 = jax.random.split(key, 5)
        q = jax.random.normal(k0, (B, S, EMBED_DIM), dtype=jnp.float32)
        k = jax.random.normal(k1, (B, S, EMBED_DIM), dtype=jnp.float32)
        v = jax.random.normal(k2, (B, S, EMBED_DIM), dtype=jnp.float32)
        Wv = jax.random.normal(k3, (EMBED_DIM, EMBED_DIM), dtype=jnp.float32) * 0.02
        bv = jnp.zeros((EMBED_DIM,), dtype=jnp.float32)
        Wo = jax.random.normal(k4, (EMBED_DIM, EMBED_DIM), dtype=jnp.float32) * 0.02
        bo = jnp.zeros((EMBED_DIM,), dtype=jnp.float32)
        return {'q': q, 'k': k, 'v': v, 'Wv': Wv, 'bv': bv, 'Wo': Wo, 'bo': bo}
    _L0_xattn_all = _L0_xattn_setup()
    _L0_xattn_in = {k: v for k, v in _L0_xattn_all.items() if k in ('Wv', 'bv', 'Wo', 'bo')}
    del _L0_xattn_all

    def _L0_ffn_setup():
        import jax, jax.numpy as jnp
        import numpy as np
        D, H, E, K = (128, 512, 8, 2)
        B, T = (2, 256)

        def _layernorm(x, g, b, eps=1e-05):
            mu = jnp.mean(x, axis=-1, keepdims=True)
            var = jnp.mean(jnp.square(x - mu), axis=-1, keepdims=True)
            return (x - mu) * jax.lax.rsqrt(var + eps) * g + b

        def _expert(x, g, b, W1, b1, W2, b2, Wo, bo):
            x = _layernorm(x, g, b)
            x1 = x @ W1 + b1
            x2 = jnp.clip(x @ W2 + b2, -20.0, 20.0)
            hidden = jnp.clip(x1 * (x2 * jax.nn.sigmoid(x2)), -10000.0, 10000.0)
            return jnp.clip(hidden @ Wo + bo, -10000.0, 10000.0)
        key = jax.random.key(seed)
        ks = jax.random.split(key, 6)
        s = 0.02
        return {'x': jax.random.normal(ks[0], (B, T, D), jnp.float32), 'ln_g': jnp.ones((D,), jnp.float32), 'ln_b': jnp.zeros((D,), jnp.float32), 'router_w': jax.random.normal(ks[1], (D, E), jnp.float32) * s, 'eg': jnp.ones((E, D), jnp.float32), 'eb': jnp.zeros((E, D), jnp.float32), 'W1': jax.random.normal(ks[2], (E, D, H), jnp.float32) * s, 'b1': jnp.zeros((E, H), jnp.float32), 'W2': jax.random.normal(ks[3], (E, D, H), jnp.float32) * s, 'b2': jnp.zeros((E, H), jnp.float32), 'Wo': jax.random.normal(ks[4], (E, H, D), jnp.float32) * s, 'bo': jnp.zeros((E, D), jnp.float32)}
    _L0_ffn_all = _L0_ffn_setup()
    _L0_ffn_in = {k: v for k, v in _L0_ffn_all.items() if k in ('ln_g', 'ln_b', 'router_w', 'eg', 'eb', 'W1', 'b1', 'W2', 'b2', 'Wo', 'bo')}
    del _L0_ffn_all
    return {'x': x, 'ctx_1024': ctx_1024, 'L0_attn_W_q': _L0_attn_in['W_q'], 'L0_attn_W_k': _L0_attn_in['W_k'], 'L0_attn_W_v': _L0_attn_in['W_v'], 'L0_attn_W_o': _L0_attn_in['W_o'], 'L0_attn_W_down_kv': _L0_attn_in['W_down_kv'], 'L0_attn_W_up_k': _L0_attn_in['W_up_k'], 'L0_attn_W_up_v': _L0_attn_in['W_up_v'], 'L0_xattn_Wv': _L0_xattn_in['Wv'], 'L0_xattn_bv': _L0_xattn_in['bv'], 'L0_xattn_Wo': _L0_xattn_in['Wo'], 'L0_xattn_bo': _L0_xattn_in['bo'], 'L0_ffn_ln_g': _L0_ffn_in['ln_g'], 'L0_ffn_ln_b': _L0_ffn_in['ln_b'], 'L0_ffn_router_w': _L0_ffn_in['router_w'], 'L0_ffn_eg': _L0_ffn_in['eg'], 'L0_ffn_eb': _L0_ffn_in['eb'], 'L0_ffn_W1': _L0_ffn_in['W1'], 'L0_ffn_b1': _L0_ffn_in['b1'], 'L0_ffn_W2': _L0_ffn_in['W2'], 'L0_ffn_b2': _L0_ffn_in['b2'], 'L0_ffn_Wo': _L0_ffn_in['Wo'], 'L0_ffn_bo': _L0_ffn_in['bo']}

def reference(x, ctx_1024, L0_attn_W_q, L0_attn_W_k, L0_attn_W_v, L0_attn_W_o, L0_attn_W_down_kv, L0_attn_W_up_k, L0_attn_W_up_v, L0_xattn_Wv, L0_xattn_bv, L0_xattn_Wo, L0_xattn_bo, L0_ffn_ln_g, L0_ffn_ln_b, L0_ffn_router_w, L0_ffn_eg, L0_ffn_eb, L0_ffn_W1, L0_ffn_b1, L0_ffn_W2, L0_ffn_b2, L0_ffn_Wo, L0_ffn_bo):
    import jax
    import jax.numpy as jnp

    def _L0_attn_ref(x, W_q, W_k, W_v, W_o, W_down_kv, W_up_k, W_up_v):
        import jax, jax.numpy as jnp
        import numpy as np
        import math
        B, S, D = (4, 256, 128)
        H = 16
        HD = D // H
        DL = 32
        LAMBDA_DECAY = 0.01
        b, s, d = x.shape
        q = x @ W_q
        k = x @ W_k
        v = x @ W_v
        latent_kv = (k + v) @ W_down_kv
        k_rec = (latent_kv @ W_up_k).reshape(b, s, H, HD).transpose(0, 2, 1, 3)
        v_rec = (latent_kv @ W_up_v).reshape(b, s, H, HD).transpose(0, 2, 1, 3)
        qh = q.reshape(b, s, H, HD).transpose(0, 2, 1, 3)
        scores = jnp.einsum('bhqd,bhkd->bhqk', qh, k_rec) / math.sqrt(d)
        t = jnp.arange(s, dtype=jnp.float32)
        decay = jnp.exp(-LAMBDA_DECAY * jnp.abs(t[:, None] - t[None, :]))
        scores = scores * decay[None, None, :, :]
        attn = jax.nn.softmax(scores, axis=-1)
        out = jnp.einsum('bhqk,bhkd->bhqd', attn, v_rec)
        out = out.transpose(0, 2, 1, 3).reshape(b, s, d)
        return out @ W_o

    def _L0_xattn_ref(q, k, v, Wv, bv, Wo, bo):
        import jax, jax.numpy as jnp
        import numpy as np
        EMBED_DIM = 128
        NUM_HEADS = 16
        HEAD_DIM = EMBED_DIM // NUM_HEADS
        B, S = (4, 512)

        def _split_heads(x):
            b, s, e = x.shape
            return x.reshape(b, s, NUM_HEADS, HEAD_DIM).transpose(0, 2, 1, 3)
        vp = v @ Wv.T + bv
        qh = _split_heads(q)
        kh = _split_heads(k)
        vh = _split_heads(vp)
        scores = jax.nn.softmax(jnp.einsum('bhsd,bhse->bhde', qh, kh) / EMBED_DIM ** 0.5, axis=-1)
        out = jnp.einsum('bhsd,bhde->bhse', vh, scores)
        out = out.transpose(0, 2, 1, 3).reshape(q.shape[0], -1, EMBED_DIM)
        return out @ Wo.T + bo

    def _L0_ffn_ref(x, ln_g, ln_b, router_w, eg, eb, W1, b1, W2, b2, Wo, bo):
        import jax, jax.numpy as jnp
        import numpy as np
        D, H, E, K = (128, 512, 8, 2)
        B, T = (2, 256)

        def _layernorm(x, g, b, eps=1e-05):
            mu = jnp.mean(x, axis=-1, keepdims=True)
            var = jnp.mean(jnp.square(x - mu), axis=-1, keepdims=True)
            return (x - mu) * jax.lax.rsqrt(var + eps) * g + b

        def _expert(x, g, b, W1, b1, W2, b2, Wo, bo):
            x = _layernorm(x, g, b)
            x1 = x @ W1 + b1
            x2 = jnp.clip(x @ W2 + b2, -20.0, 20.0)
            hidden = jnp.clip(x1 * (x2 * jax.nn.sigmoid(x2)), -10000.0, 10000.0)
            return jnp.clip(hidden @ Wo + bo, -10000.0, 10000.0)
        Bb, Tt, Dd = x.shape
        xf = _layernorm(x.reshape(-1, Dd), ln_g, ln_b)
        N = xf.shape[0]
        logits = xf @ router_w
        scores, idx = jax.lax.top_k(logits, K)
        gate = jax.nn.softmax(scores, axis=-1)
        gates_e = jnp.zeros((N, E), xf.dtype).at[jnp.arange(N)[:, None], idx].add(gate)

        def body(acc, p):
            gcol, g, b, w1, bb1, w2, bb2, wo, bbo = p
            return (acc + gcol[:, None] * _expert(xf, g, b, w1, bb1, w2, bb2, wo, bbo), None)
        out, _ = jax.lax.scan(body, jnp.zeros_like(xf), (gates_e.T, eg, eb, W1, b1, W2, b2, Wo, bo))
        return out.reshape(Bb, Tt, Dd)
    x = _layernorm(x + _L0_attn_ref(x, L0_attn_W_q, L0_attn_W_k, L0_attn_W_v, L0_attn_W_o, L0_attn_W_down_kv, L0_attn_W_up_k, L0_attn_W_up_v), axis=-1)
    x = _layernorm(x + _L0_xattn_ref(x, ctx_1024, ctx_1024, L0_xattn_Wv, L0_xattn_bv, L0_xattn_Wo, L0_xattn_bo), axis=-1)
    x = _layernorm(x + _L0_ffn_ref(x, L0_ffn_ln_g, L0_ffn_ln_b, L0_ffn_router_w, L0_ffn_eg, L0_ffn_eb, L0_ffn_W1, L0_ffn_b1, L0_ffn_W2, L0_ffn_b2, L0_ffn_Wo, L0_ffn_bo), axis=-1)
    return x

_drawn_inputs = setup_inputs


def setup_inputs(seed=0):
    import zlib

    import numpy as np

    out = dict(_drawn_inputs(seed))
    spreads = {'L0_xattn_bv': (0.0, 0.498),
     'L0_xattn_bo': (0.0, 0.1),
     'L0_ffn_ln_g': (1.0, 0.2),
     'L0_ffn_ln_b': (0.0, 0.336),
     'L0_ffn_eg': (1.0, 0.6),
     'L0_ffn_eb': (0.0, 0.8),
     'L0_ffn_b1': (0.0, 0.8),
     'L0_ffn_b2': (0.0, 0.8),
     'L0_ffn_bo': (0.0, 0.695)}
    factors = {'L0_ffn_W1': 5.59, 'L0_ffn_W2': 5.62, 'L0_ffn_Wo': 5.157}
    for name, (base, spread) in spreads.items():
        noise = np.random.default_rng([zlib.crc32(name.encode()), seed]).standard_normal(out[name].shape)
        drawn = base * np.exp(spread * noise) if base else spread * noise
        out[name] = jnp.asarray(drawn.astype(out[name].dtype))
    for name, factor in factors.items():
        out[name] = (out[name] * factor).astype(out[name].dtype)
    return out
```

```python
from contextlib import ExitStack

import concourse.bass as bass
from concourse import mybir

F32 = mybir.dt.float32
I32 = mybir.dt.int32
U32 = mybir.dt.uint32
ALU = mybir.AluOpType
ACT = mybir.ActivationFunctionType
AX = mybir.AxisListType

P = 128
EPS = 1e-5
LAMBDA = 0.01
NEG = -3.0e38


def decoder_layer(nc, x, ctx_in, W_q, W_k, W_v, W_o, W_down, W_upk, W_upv, xWv, xbv, xWo, xbo,
                  ln_g, ln_b, router, eg, eb, W1, b1, W2, b2, Wo, bo, out):
    B, S, D = x.shape
    assert S == P and D == P
    H = 16
    HD = D // H
    DL = W_down.shape[1]
    HALF = H // 2
    E, _, HID = W1.shape
    CH = HID // P
    VW = D + H
    SCALE = float(D) ** -0.5
    TILE = 2 * P
    N = B * S
    TILES = 2 * N // TILE + E - 1
    SLOTS = TILES * TILE
    MAXT = N // TILE
    PRM = 2 + 2 * CH
    LOAD = 8

    xs_dram = nc.dram_tensor("expert_in", [SLOTS, D], F32)
    ys_dram = nc.dram_tensor("expert_out", [SLOTS, D], F32)

    GH = 32 // HD
    KIMG_H = HD * GH * S + S
    KIMG = GH * KIMG_H * (P // 32)
    kimg = nc.dram_tensor("key_image", [2, KIMG], F32)

    with ExitStack() as es:
        def sb(name, shape, dt=F32):
            return es.enter_context(nc.sbuf_tensor(name, shape, dt))

        def sem(name):
            return es.enter_context(nc.semaphore(name))

        xall = sb("xall", [P, B, D])
        call = sb("call", [P, B, D])
        xf = sb("xf", [P, 2, D])
        gain_row = sb("gain_row", [P, D])
        offset_row = sb("offset_row", [P, D])
        rpad = sb("rpad", [P, P])
        xfT = sb("xfT", [P, S])
        logits = sb("logits", [P, B, E])
        st3 = sb("st3", [P, 6]); mv3 = sb("mv3", [P, 2]); rs3 = sb("rs3", [P, 1])
        st4 = sb("st4", [P, 6]); mv4 = sb("mv4", [P, 2]); rs4 = sb("rs4", [P, 1])
        xn = sb("xn", [P, D])
        params = sb("params", [P, E, PRM])
        bo_rows = sb("bo_rows", [P, E, D])
        ident = sb("ident", [P, P])
        decay = sb("decay", [P, P])
        wq = sb("wq", [P, D])
        wo = sb("wo", [P, D])
        wkf = sb("wkf", [P, D])
        wvf = sb("wvf", [P, D])
        xwvT = sb("xwvT", [P, D])
        xwoT = sb("xwoT", [P, D])
        bv_col = sb("bv_col", [P, 1])
        bo_row = sb("bo_row", [P, D])
        blkneg = sb("blkneg", [P, H, HD])
        mhalf = sb("mhalf", [P, 4])
        eps_col = sb("eps_col", [P, 4])
        setup = sb("setup", [P, 8, D])
        xin = sb("xin", [P, 2, D])
        cin = sb("cin", [P, 2, D])
        x1 = sb("x1", [P, 2, D])
        xT = sb("xT", [P, 2, S])
        qT = sb("qT", [P, 2, S])
        kT = sb("kT", [P, 2, S])
        kbd = sb("kbd", [P, 2, H, S])
        vbd = sb("vbd", [P, 2, H, VW])
        sc = sb("sc", [P, 4, HALF, S])
        rowmax = sb("rowmax", [P, 4, HALF])
        pT = sb("pT", [P, 4, 4 * S])
        rsum = sb("rsum", [P, 2, H])
        att = sb("att", [P, D])
        attT = sb("attT", [P, D])
        res1 = sb("res1", [P, D])
        st1 = sb("st1", [P, 6])
        mv1 = sb("mv1", [P, 2])
        rs1 = sb("rs1", [P, 1])
        cT = sb("cT", [P, S])
        vpT = sb("vpT", [P, S])
        gm = sb("gm", [P, D])
        gmax = sb("gmax", [P, 1])
        gsum = sb("gsum", [P, 1])
        gex = sb("gex", [P, D])
        gA = sb("gA", [P, D])
        oT = sb("oT", [P, S])
        res2 = sb("res2", [P, D])
        st2 = sb("st2", [P, 6])
        mv2 = sb("mv2", [P, 2])
        rs2 = sb("rs2", [P, 1])

        zrow = sb("zrow", [P, 4 * D])
        ps_s = es.enter_context(nc.psum_tensor("ps_s", [P, 2, 4, S], F32))
        ps_t = es.enter_context(nc.psum_tensor("ps_t", [P, 2, 512], F32))
        ps_a = es.enter_context(nc.psum_tensor("ps_a", [P, 512], F32))
        ps_m = es.enter_context(nc.psum_tensor("ps_m", [P, 3, 4, P], F32))
        acc = ps_a[:, 0:VW]
        m0a, m0b = ps_m[:, 0, 0, :], ps_m[:, 0, 1, :]
        m1a, m1b = ps_m[:, 1, 0, :], ps_m[:, 1, 1, :]
        m2a, m2b = ps_m[:, 2, 0, :], ps_m[:, 2, 1, :]
        m0c, m2c = ps_m[:, 0, 2, :], ps_m[:, 2, 2, :]

        ld_w = sem("ld_w"); ld_x = sem("ld_x"); ld_c = sem("ld_c"); zeroed = sem("zeroed")
        x_in = [sem("x_in0"), sem("x_in1")]; c_in = [sem("c_in0"), sem("c_in1")]
        cst = sem("cst"); su_v = sem("su_v"); su_p = sem("su_p"); su_a = sem("su_a")
        x_trans = sem("x_trans"); xT_ready = sem("xT_ready")
        qk_done = sem("qk_done"); q_ready = sem("q_ready"); k_ready = sem("k_ready")
        v_done = sem("v_done"); v_ready = sem("v_ready")
        k_clear = sem("k_clear"); k_stored = [sem("k_stored0"), sem("k_stored1")]
        k_spread = [sem("k_spread0"), sem("k_spread1")]
        scored = sem("scored"); decayed = sem("decayed"); maxed = sem("maxed")
        shifted = sem("shifted"); exped = sem("exped")
        p_trans = sem("p_trans"); pT_ready = sem("pT_ready"); mixed = sem("mixed")
        sums_inv = sem("sums_inv"); att_ready = sem("att_ready"); att_trans = sem("att_trans")
        attT_ready = sem("attT_ready"); projected = sem("projected"); res1_ready = sem("res1_ready")
        stat1 = sem("stat1"); mean1 = sem("mean1"); rstd1 = sem("rstd1"); x1_ready = sem("x1_ready")
        c_trans = sem("c_trans"); cT_ready = sem("cT_ready"); vp_done = sem("vp_done"); vpT_ready = sem("vpT_ready")
        gram = sem("gram"); gm_ready = sem("gm_ready"); gmax_ready = sem("gmax_ready"); gexp = sem("gexp")
        ginv = sem("ginv"); gA_ready = sem("gA_ready")
        o_done = sem("o_done"); oT_ready = sem("oT_ready"); x_out = sem("x_out")
        res2a = sem("res2a"); res2_ready = sem("res2_ready"); stat2 = sem("stat2"); mean2 = sem("mean2"); rstd2 = sem("rstd2")
        x2_ready = sem("x2_ready")
        stat3 = sem("stat3"); mean3 = sem("mean3"); rstd3 = sem("rstd3"); xn_ready = sem("xn_ready")
        gained = sem("gained"); xf_ready = sem("xf_ready")
        stat4 = sem("stat4"); mean4 = sem("mean4"); rstd4 = sem("rstd4"); xhat_ready = sem("xhat_ready")
        f_trans = sem("f_trans"); fT_ready = sem("fT_ready"); routed = sem("routed"); logits_ready = sem("logits_ready")
        ld_p = sem("ld_p"); ld_e = sem("ld_e"); zero_row = sem("zero_row"); cleared = sem("cleared")

        held = {"DVE": sem("held_dve")}
        eps1, eps2, eps3, eps4, eps5 = (sem(f"eps{i}") for i in range(1, 6))

        def hold(eng, s, v):
            eng.wait_ge(s, v)
            eng.sem_inc(held[eng.engine.name], 1)

        def on(b, lag):
            return not isinstance(b, int) or 0 <= b - lag < B

        def before(eng, s, v):
            if not isinstance(v, int) or v > 0:
                eng.wait_ge(s, v)

        def at(t, b):
            return t[:, b, :] if isinstance(b, int) else t[:, bass.ds(b, 1), :].rearrange("p a n -> p (a n)")

        def steps(eng, step):
            for b in range(-1, 8):
                step(b, b % 2)
            with eng.Fori(0, (B - 10) // 2) as pair:
                step(2 * pair + 8, 0)
                step(2 * pair + 9, 1)
            for b in range(B - 2, B + 6):
                step(b, b % 2)

        wsrc = [W_q, W_k, W_v, W_o, xWv, xWo]

        with nc.Block() as block:

            @block.sync
            def _(sp):
                for i, w in enumerate(wsrc):
                    sp.dma_start([wq[:, :], setup[:, 0, :], setup[:, 1, :], wo[:, :], setup[:, 2, :],
                                  setup[:, 3, :]][i], w).then_inc(ld_w, 16)
                sp.dma_start(setup[:, 4, 0:DL], W_down).then_inc(ld_w, 16)
                sp.dma_start(setup[0:DL, 5, :], W_upk).then_inc(ld_w, 16)
                sp.dma_start(setup[0:DL, 6, :], W_upv).then_inc(ld_w, 16)
                sp.dma_start(bv_col[:, :], xbv.rearrange("(p a) -> p a", a=1)).then_inc(ld_w, 16)
                sp.dma_start(bo_row[:, :], xbo.rearrange("(a n) -> a n", a=1).to_broadcast([P, D])).then_inc(ld_w, 16)
                sp.dma_start(xin[:, 0, :], x[0]).then_inc(x_in[0], 16)
                for dst, src, done in ((xall, x, ld_x), (call, ctx_in, ld_c)):
                    for i in range(0, B, LOAD):
                        sp.dma_start(dst[:, i:i + LOAD, :], src[i:i + LOAD].rearrange("b s d -> s b d")).then_inc(done, 16)
                sp.dma_start(gain_row[:, :], ln_g.rearrange("(a n) -> a n", a=1).to_broadcast([P, D])).then_inc(ld_p, 16)
                sp.dma_start(offset_row[:, :], ln_b.rearrange("(a n) -> a n", a=1).to_broadcast([P, D])).then_inc(ld_p, 16)
                sp.wait_ge(zero_row, 3)
                sp.dma_start(rpad[:, 0:E], router).then_inc(ld_p, 16)
                for i in range(2):
                    flat = kimg[i].rearrange("(p n) -> p n", p=P)
                    for j in range(0, KIMG // P, 4 * D):
                        n = min(4 * D, KIMG // P - j)
                        sp.dma_start(flat[:, j:j + n], zrow[:, 0:n]).then_inc(k_clear, 16)
                sp.wait_ge(k_clear, 32 * (-(-(KIMG // P) // (4 * D))))
                sp.wait_ge(cst, 5)

                def dram(t, n):
                    return t[n] if isinstance(n, int) else t[bass.ds(n, 1)].rearrange("a s d -> (a s) d")

                def step(b, par):
                    if on(b, -2):
                        before(sp, x_trans, b + 1)
                        sp.dma_start(xin[:, par, :], dram(x, b + 2)).then_inc(x_in[par], 16)
                    if on(b, 2):
                        before(sp, c_trans, b - 3)
                        sp.dma_start(cin[:, par, :], dram(ctx_in, b - 2)).then_inc(c_in[par], 16)
                    if on(b, -1):
                        n = b + 1
                        q = 1 - par
                        sp.wait_ge(k_ready, n + 1)
                        before(sp, scored, 4 * (b - 1) + 4)
                        img = kimg[q]
                        sp.dma_start(bass.AP(img.tensor, img.offset, [[KIMG_H, H], [GH * S, HD], [1, S]]),
                                     kT[:, q, :]).then_inc(k_stored[q], 16)
                        sp.wait_ge(k_stored[q], 8 * (n - q) + 16)
                        for g in range(P // 32):
                            rows = bass.AP(img.tensor, img.offset + g * GH * KIMG_H, [[GH * S, 32], [1, GH * S]])
                            sp.dma_start(kbd[32 * g:32 * g + 32, q, GH * g:GH * g + GH, :],
                                         rows).then_inc(k_spread[q], 16)
                steps(sp, step)

            @block.gpsimd
            def _(pool):
                pool.memset(ident[:, :], 0.0).then_inc(cst, 1)
                pool.wait_ge(cst, 1)
                pool.affine_select(out=ident[:, :], in_=ident[:, :], compare_op=ALU.not_equal, fill=1.0,
                                   base=0, pattern=[[-1, P]], channel_multiplier=1).then_inc(cst, 1)
                pool.memset(blkneg[:, :, :], 0.0).then_inc(cst, 1)
                pool.memset(mhalf[:, :], -0.5).then_inc(cst, 1)
                pool.memset(eps_col[:, :], EPS).then_inc(zero_row, 1)
                pool.memset(kbd[:, :, :, :], 0.0).then_inc(cst, 1)
                pool.wait_ge(cst, 3)
                pool.affine_select(out=blkneg[:, :, :], in_=blkneg[:, :, :], compare_op=ALU.is_ge, fill=NEG,
                                   base=0, pattern=[[-HD, H], [0, HD]], channel_multiplier=1).then_inc(cst, 1)
                pool.wait_ge(cst, 6)
                pool.affine_select(out=blkneg[:, :, :], in_=blkneg[:, :, :], compare_op=ALU.is_ge, fill=NEG,
                                   base=HD - 1, pattern=[[HD, H], [0, HD]], channel_multiplier=-1).then_inc(cst, 1)
                pool.iota(setup[:, 7, :].bitcast(I32), pattern=[[-1, P]], base=0, channel_multiplier=1).then_inc(cst, 1)

                pool.memset(zrow[:, :], 0.0).then_inc(zero_row, 1)
                pool.memset(rpad[:, :], 0.0).then_inc(zero_row, 1)
                pool.wait_ge(zero_row, 3)
                for i in range(SLOTS // (4 * P)):
                    pool.dma_start(xs_dram[4 * P * i:4 * P * (i + 1), :].rearrange("(p a) d -> p (a d)", p=P),
                                   zrow[:, :]).then_inc(cleared, 16)
                if SLOTS % (4 * P):
                    pool.dma_start(xs_dram[SLOTS - SLOTS % (4 * P):SLOTS, :].rearrange("(p a) d -> p (a d)", p=P),
                                   zrow[:, 0:SLOTS % (4 * P)]).then_inc(cleared, 16)
                with nc.allow_non_contiguous_dma(reason="parameters of one element per partition, once"):
                    pool.dma_start(params[:, :, 0:1], eg.rearrange("e (p a) -> p e a", a=1)).then_inc(ld_e, 16)
                    pool.dma_start(params[:, :, 1:2], eb.rearrange("e (p a) -> p e a", a=1)).then_inc(ld_e, 16)
                    pool.dma_start(params[:, :, 2:2 + CH], b1.rearrange("e (p c) -> p e c", c=CH)).then_inc(ld_e, 16)
                    pool.dma_start(params[:, :, 2 + CH:PRM], b2.rearrange("e (p c) -> p e c", c=CH)).then_inc(ld_e, 16)
                pool.dma_start(bo_rows[:, :, :], bo.rearrange("(a e) d -> a e d", a=1).to_broadcast([P, E, D])).then_inc(ld_e, 16)

                def rstd(mean, count, rs, mv, added, done):
                    pool.wait_ge(mean, count)
                    pool.tensor_tensor(rs[:, :], mv[:, 1:2], eps_col[:, 0:1], ALU.add).then_inc(added, 1)
                    pool.wait_ge(added, count)
                    pool.tensor_tensor(rs[:, :], rs[:, :], mhalf[:, 0:1], ALU.pow).then_inc(done, 1)

                def shift(b, half, slot):
                    k = 2 * b + half + 1
                    pool.wait_ge(maxed, k)
                    pool.tensor_tensor(sc[:, slot], sc[:, slot],
                                       rowmax[:, slot, :].unsqueeze(2).to_broadcast([P, HALF, S]),
                                       ALU.subtract).then_inc(shifted, 1)

                def step(b, par):
                    if on(b, 4):
                        rstd(mean2, b - 4 + 1, rs2, mv2, eps2, rstd2)
                    if on(b, 5):
                        rstd(mean3, b - 5 + 1, rs3, mv3, eps3, rstd3)
                    if on(b, 6):
                        rstd(mean4, b - 6 + 1, rs4, mv4, eps4, rstd4)
                    if on(b, 0):
                        shift(b, 0, 2 * par)
                    if on(b, 2):
                        rstd(mean1, b - 2 + 1, rs1, mv1, eps1, rstd1)
                    if on(b, 5):
                        pool.wait_ge(ld_p, 16 * 3)
                        pool.wait_ge(xn_ready, b - 5 + 1)
                        pool.tensor_tensor(xn[:, :], xn[:, :], gain_row[:, :], ALU.mult).then_inc(gained, 1)
                        pool.wait_ge(gained, b - 5 + 1)
                        pool.tensor_tensor(xf[:, 1 - par, :], xn[:, :], offset_row[:, :], ALU.add).then_inc(xf_ready, 1)
                    if on(b, 0):
                        shift(b, 1, 2 * par + 1)
                steps(pool, step)

            @block.tensor
            def _(pe):
                pe.wait_ge(ld_w, 16 * 11)
                pe.wait_ge(cst, 2)
                pe.wait_ge(su_v, 1)
                pe.transpose(m0a, setup[:, 0, :], ident[:, :]).then_inc(su_p, 1)
                pe.transpose(m1a, setup[:, 2, :], ident[:, :]).then_inc(su_p, 1)
                pe.transpose(m2a, setup[:, 3, :], ident[:, :]).then_inc(su_p, 1)
                pe.wait_ge(su_a, 1)
                pe.matmul(ps_m[0:DL, 0, 0, :], setup[:, 4, 0:DL], setup[:, 1, :], start=True, stop=True).then_inc(su_p, 1)
                pe.wait_ge(su_a, 4)
                pe.matmul(m1a, setup[0:DL, 0, :], setup[0:DL, 5, :], start=True, stop=True).then_inc(su_p, 1)
                pe.matmul(m2a, setup[0:DL, 0, :], setup[0:DL, 6, :], start=True, stop=True).then_inc(su_p, 1)
                pe.wait_ge(su_a, 6)

                def p_transposes(b, quarter, par):
                    k = 4 * b + quarter + 1
                    if quarter % 2 == 0:
                        pe.wait_ge(exped, 2 * b + quarter // 2 + 1)
                    before(pe, pT_ready, k - 2)
                    for j in range(4):
                        mm = pe.transpose(ps_t[:, quarter % 2, j * S:(j + 1) * S],
                                          sc[:, 2 * par + quarter // 2, 4 * (quarter % 2) + j, :], ident[:, :])
                    mm.then_inc(p_trans, 1)

                def p_mix(b, quarter, par):
                    pe.wait_ge(pT_ready, 4 * b + quarter + 1)
                    if quarter == 0:
                        pe.wait_ge(v_ready, b + 1)
                        before(pe, att_ready, b)
                    for j in range(4):
                        h = 4 * quarter + j
                        mm = pe.matmul(acc, pT[:, quarter, j * S:(j + 1) * S], vbd[:, par, h, :],
                                       start=(h == 0), stop=(h == H - 1))
                    mm.then_inc(mixed, 1)

                def p_score(b, quarter, par):
                    if quarter == 0:
                        pe.wait_ge(k_spread[par], 32 * (b - par) + 64)
                        pe.wait_ge(q_ready, b + 1)
                    before(pe, decayed, 4 * b + quarter - 1)
                    pe.matmul(ps_s[:, quarter % 2, :, :], qT[:, par, :], kbd[:, par, 4 * quarter:4 * quarter + 4, :],
                              start=True, stop=True).then_inc(scored, 1)

                def step(b, par):
                    if on(b, 3):
                        pe.wait_ge(res1_ready, b - 3 + 1)
                    if on(b, -1):
                        pe.wait_ge(x_in[1 - par], 8 * (b + par) + 16)
                        pe.transpose(m0a, xin[:, 1 - par, :], ident[:, :]).then_inc(x_trans, 1)
                    if on(b, 3):
                        pe.wait_ge(c_in[1 - par], 8 * (b - 4 + par) + 16)
                        pe.transpose(m0b, cin[:, 1 - par, :], ident[:, :]).then_inc(c_trans, 1)
                    if on(b, 6):
                        pe.wait_ge(xf_ready, b - 6 + 1)
                        pe.transpose(m0c, xf[:, par, :], ident[:, :]).then_inc(f_trans, 1)
                    if on(b, 0):
                        p_score(b, 0, par)
                    if on(b, -1):
                        pe.wait_ge(xT_ready, b + 2)
                        before(pe, oT_ready, b - 3)
                        pe.matmul(m1a, wq[:, :], xT[:, 1 - par, :], start=True, stop=True)
                        pe.matmul(m1b, wkf[:, :], xT[:, 1 - par, :], start=True, stop=True).then_inc(qk_done, 1)
                    if on(b, 0):
                        p_score(b, 1, par)
                    before(pe, res2a, b - 3 if on(b, 4) else 0)
                    if on(b, 0):
                        pe.matmul(m2a, xT[:, par, :], wvf[:, :], start=True, stop=True).then_inc(v_done, 1)
                    if on(b, 3):
                        pe.wait_ge(x1_ready, b - 3 + 1)
                        pe.wait_ge(ld_c, 16 * B // LOAD)
                        pe.matmul(m2b, x1[:, 1 - par, :], at(call, b - 3), start=True, stop=True).then_inc(gram, 1)
                    if on(b, 6):
                        pe.wait_ge(fT_ready, b - 6 + 1)
                        pe.matmul(m2c, xfT[:, :], rpad[:, :], start=True, stop=True).then_inc(routed, 1)
                    if on(b, 1):
                        p_transposes(b - 1, 0, 1 - par)
                        p_transposes(b - 1, 1, 1 - par)
                    if on(b, -1):
                        pe.wait_ge(xT_ready, b + 2)
                    if on(b, 3):
                        pe.wait_ge(cT_ready, b - 3 + 1)
                    if on(b, 6):
                        pe.wait_ge(fT_ready, b - 6 + 1)
                    if on(b, 2):
                        pe.wait_ge(att_ready, b - 2 + 1)
                        pe.transpose(m0a, att[:, :], ident[:, :]).then_inc(att_trans, 1)
                    if on(b, 3):
                        pe.matmul(m0b, xwvT[:, :], cT[:, :], start=True, stop=True).then_inc(vp_done, 1)
                    if on(b, 1):
                        p_mix(b - 1, 0, 1 - par)
                    if on(b, 0):
                        p_score(b, 2, par)
                    if on(b, 1):
                        p_mix(b - 1, 1, 1 - par)
                    if on(b, 2):
                        pe.wait_ge(attT_ready, b - 2 + 1)
                        if on(b, 3):
                            pe.wait_ge(vpT_ready, b - 3 + 1)
                        pe.matmul(m0a, attT[:, :], wo[:, :], start=True, stop=True).then_inc(projected, 1)
                    if on(b, 0):
                        p_score(b, 3, par)
                    if on(b, 1):
                        p_transposes(b - 1, 2, 1 - par)
                    if on(b, 3):
                        pe.wait_ge(gA_ready, b - 3 + 1)
                        pe.wait_ge(vpT_ready, b - 3 + 1)
                        if on(b, -1):
                            pe.wait_ge(k_ready, b + 2)
                        pe.matmul(m1a, gA[:, :], vpT[:, :], start=True, stop=True).then_inc(o_done, 1)
                    if on(b, 1):
                        p_transposes(b - 1, 3, 1 - par)
                        p_mix(b - 1, 2, 1 - par)
                    if on(b, 3):
                        pe.wait_ge(oT_ready, b - 3 + 1)
                        if on(b, 0):
                            pe.wait_ge(v_ready, b + 1)
                        if on(b, 6):
                            pe.wait_ge(logits_ready, b - 6 + 1)
                        pe.matmul(m2a, oT[:, :], xwoT[:, :], start=True, stop=True).then_inc(x_out, 1)
                    if on(b, 1):
                        p_mix(b - 1, 3, 1 - par)
                steps(pe, step)

            @block.scalar
            def _(act):
                def copy(out, in_):
                    return act.activation(out, in_, ACT.Copy)
                act.wait_ge(su_p, 1)
                copy(setup[:, 1, :], m0a).then_inc(su_a, 1)
                act.wait_ge(su_p, 3)
                copy(xwvT[:, :], m1a).then_inc(su_a, 1)
                copy(xwoT[:, :], m2a).then_inc(su_a, 1)
                act.wait_ge(su_p, 4)
                copy(setup[0:DL, 0, :], ps_m[0:DL, 0, 0, :]).then_inc(su_a, 1)
                act.wait_ge(su_p, 6)
                copy(wkf[:, :], m1a).then_inc(su_a, 1)
                copy(wvf[:, :], m2a).then_inc(su_a, 1)
                act.wait_ge(su_v, 4)
                act.activation(decay[:, :], setup[:, 7, :], ACT.Exp, scale=-LAMBDA).then_inc(su_a, 1)

                def a_exp(b, half, slot):
                    act.wait_ge(shifted, 2 * b + half + 1)
                    act.activation(sc[:, slot], sc[:, slot], ACT.Exp).then_inc(exped, 1)

                def a_pT(b, quarter):
                    k = 4 * b + quarter + 1
                    act.wait_ge(p_trans, k)
                    before(act, mixed, k - 4)
                    copy(pT[:, quarter, :], ps_t[:, quarter % 2, :]).then_inc(pT_ready, 1)

                def step(b, par):
                    if on(b, -1):
                        act.wait_ge(x_trans, b + 2)
                        before(act, v_done, b)
                        if on(b, 3):
                            act.wait_ge(c_trans, b - 3 + 1)
                        if on(b, 6):
                            act.wait_ge(f_trans, b - 6 + 1)
                        copy(xT[:, 1 - par, :], m0a).then_inc(xT_ready, 1)
                    if on(b, 3):
                        act.wait_ge(c_trans, b - 3 + 1)
                        if on(b, 6):
                            act.wait_ge(f_trans, b - 6 + 1)
                        before(act, vp_done, b - 3)
                        copy(cT[:, :], m0b).then_inc(cT_ready, 1)
                    if on(b, 6):
                        act.wait_ge(f_trans, b - 6 + 1)
                        before(act, routed, b - 6)
                        copy(xfT[:, :], m0c).then_inc(fT_ready, 1)
                    if on(b, 1):
                        a_exp(b - 1, 1, 2 * (1 - par) + 1)
                    if on(b, -1):
                        act.wait_ge(qk_done, b + 2)
                        before(act, scored, 4 * (b - 1) + 4)
                        copy(qT[:, 1 - par, :], m1a).then_inc(q_ready, 1)
                        before(act, k_stored[1 - par], 8 * (b - 1 - (1 - par)) + 16)
                        copy(kT[:, 1 - par, :], m1b).then_inc(k_ready, 1)
                    if on(b, 1):
                        a_pT(b - 1, 0)
                        a_pT(b - 1, 1)
                    if on(b, 2):
                        act.wait_ge(att_trans, b - 2 + 1)
                        before(act, projected, b - 2)
                        if on(b, 3):
                            act.wait_ge(vp_done, b - 3 + 1)
                        copy(attT[:, :], m0a).then_inc(attT_ready, 1)
                    if on(b, 3):
                        act.wait_ge(vp_done, b - 3 + 1)
                        before(act, o_done, b - 3)
                        act.activation(vpT[:, :], m0b, ACT.Identity, bias=bv_col[:, 0:1]).then_inc(vpT_ready, 1)
                        act.wait_ge(gmax_ready, b - 3 + 1)
                        act.activation(gex[:, :], gm[:, :], ACT.Exp, bias=gmax[:, 0:1],
                                       accum_out=gsum[:, 0:1]).then_inc(gexp, 1)
                    if on(b, 0):
                        a_exp(b, 0, 2 * par)
                    if on(b, 1):
                        a_pT(b - 1, 2)
                        a_pT(b - 1, 3)
                    if on(b, 3):
                        act.wait_ge(o_done, b - 3 + 1)
                        before(act, x_out, b - 3)
                        copy(oT[:, :], m1a).then_inc(oT_ready, 1)
                steps(act, step)

            @block.vector
            def _(dve):
                dve.wait_ge(ld_w, 16 * 11)
                dve.tensor_tensor(setup[:, 0, :], setup[:, 0, :], setup[:, 1, :], ALU.add).then_inc(su_v, 1)
                dve.wait_ge(cst, 8)
                dve.tensor_copy(gm[:, :], setup[:, 7, :].bitcast(I32)).then_inc(su_v, 1)
                dve.memset(vbd[:, :, :, :], 0.0).then_inc(su_v, 1)
                dve.wait_ge(su_v, 3)
                dve.scalar_tensor_tensor(out=setup[:, 7, :], in0=gm[:, :], scalar=-1.0, in1=gm[:, :],
                                         op0=ALU.mult, op1=ALU.max).then_inc(su_v, 1)
                for i in range(2):
                    for h in range(H):
                        dve.memset(vbd[:, i, h, D + h:D + h + 1], 1.0).then_inc(su_v, 1)
                dve.wait_ge(su_v, 4 + 2 * H)
                dve.wait_ge(su_a, 7)
                dve.tensor_scalar(decay[:, :], decay[:, :], SCALE, None, ALU.mult).then_inc(su_v, 1)
                dve.wait_ge(su_v, 5 + 2 * H)

                def v_decay(b, quarter, par):
                    slot = 2 * par + quarter // 2
                    dve.wait_ge(scored, 4 * b + quarter + 1)
                    before(dve, p_trans, 4 * (b - 2) + quarter + 1)
                    j = 4 * (quarter % 2)
                    dve.tensor_tensor(sc[:, slot, j:j + 4, :], ps_s[:, quarter % 2, :, :],
                                      decay[:, :].unsqueeze(1).to_broadcast([P, 4, S]), ALU.mult).then_inc(decayed, 1)

                def v_max(b, half, par):
                    slot = 2 * par + half
                    dve.wait_ge(decayed, 4 * b + 2 * half + 2)
                    dve.tensor_reduce(rowmax[:, slot, :], sc[:, slot], AX.X, ALU.max).then_inc(maxed, 1)

                def step(b, par):
                    if on(b, 2):
                        dve.wait_ge(mixed, 4 * (b - 2) + 4)
                        dve.reciprocal(rsum[:, par, :], acc[:, D:VW]).then_inc(sums_inv, 1)
                    if on(b, 4):
                        dve.wait_ge(x_out, b - 4 + 1)
                        dve.tensor_tensor(res2[:, :], m2a, x1[:, par, :], ALU.add).then_inc(res2a, 1)
                    if on(b, 2):
                        dve.wait_ge(sums_inv, b - 2 + 1)
                        before(dve, att_trans, b - 2)
                        dve.tensor_tensor(att[:, :].rearrange("p (h d) -> p h d", h=H),
                                          acc[:, 0:D].rearrange("p (h d) -> p h d", h=H),
                                          rsum[:, par, :].unsqueeze(2).to_broadcast([P, H, HD]),
                                          ALU.mult).then_inc(att_ready, 1)
                    if on(b, 4):
                        dve.wait_ge(res2a, b - 4 + 1)
                        dve.tensor_tensor(res2[:, :], res2[:, :], bo_row[:, :], ALU.add).then_inc(res2_ready, 1)
                    if on(b, 0):
                        v_decay(b, 0, par)
                    if on(b, 4):
                        dve.wait_ge(res2_ready, b - 4 + 1)
                        dve.bn_stats(st2[:, :], res2[:, :]).then_inc(stat2, 1)
                    if on(b, 0):
                        v_decay(b, 1, par)
                    if on(b, 4):
                        hold(dve, stat2, b - 4 + 1)
                        dve.bn_aggr(mv2[:, :], st2[:, :]).then_inc(mean2, 1)
                    if on(b, 5):
                        hold(dve, x2_ready, b - 5 + 1)
                        dve.bn_stats(st3[:, :], at(xall, b - 5)).then_inc(stat3, 1)
                    if on(b, 6):
                        dve.wait_ge(xf_ready, b - 6 + 1)
                        dve.bn_stats(st4[:, :], xf[:, par, :]).then_inc(stat4, 1)
                    if on(b, 3):
                        dve.wait_ge(gram, b - 3 + 1)
                    if on(b, 6):
                        dve.wait_ge(routed, b - 6 + 1)
                    if on(b, 0):
                        dve.wait_ge(v_done, b + 1)
                        before(dve, mixed, 4 * (b - 2) + 4)
                        full = vbd[:, par, :, :].rearrange("p h w -> p (h w)")
                        diag = bass.AP(full.tensor, full.offset, [list(full.ap[0]), [VW + HD, H], [1, HD]])
                        dve.tensor_copy(diag, m2a.rearrange("p (h d) -> p h d", h=H)).then_inc(v_ready, 1)
                    if on(b, 3):
                        before(dve, gexp, b - 3)
                        dve.scalar_tensor_tensor(out=gm[:, :], in0=m2b, scalar=SCALE,
                                                 in1=blkneg[:, :, :].rearrange("p h d -> p (h d)"),
                                                 op0=ALU.mult, op1=ALU.add).then_inc(gm_ready, 1)
                    if on(b, 6):
                        dve.tensor_copy(at(logits, b - 6), m2c[:, 0:E]).then_inc(logits_ready, 1)
                    if on(b, 5):
                        hold(dve, stat3, b - 5 + 1)
                        dve.bn_aggr(mv3[:, :], st3[:, :]).then_inc(mean3, 1)
                    if on(b, 6):
                        hold(dve, stat4, b - 6 + 1)
                        dve.bn_aggr(mv4[:, :], st4[:, :]).then_inc(mean4, 1)
                    if on(b, 0):
                        v_max(b, 0, par)
                    if on(b, 3):
                        dve.wait_ge(gm_ready, b - 3 + 1)
                        dve.tensor_reduce(gmax[:, :], gm[:, :], AX.X, ALU.max, negate=True).then_inc(gmax_ready, 1)
                    if on(b, 4):
                        dve.wait_ge(rstd2, b - 4 + 1)
                        dve.tensor_scalar(at(xall, b - 4), res2[:, :], mv2[:, 0:1], rs2[:, 0:1],
                                          ALU.subtract, ALU.mult).then_inc(x2_ready, 1)
                    if on(b, 5):
                        dve.wait_ge(rstd3, b - 5 + 1)
                        before(dve, xf_ready, b - 5)
                        dve.tensor_scalar(xn[:, :], at(xall, b - 5), mv3[:, 0:1], rs3[:, 0:1],
                                          ALU.subtract, ALU.mult).then_inc(xn_ready, 1)
                    if on(b, 6):
                        dve.wait_ge(rstd4, b - 6 + 1)
                        dve.tensor_scalar(at(call, b - 6), xf[:, par, :], mv4[:, 0:1], rs4[:, 0:1],
                                          ALU.subtract, ALU.mult).then_inc(xhat_ready, 1)
                    if on(b, 0):
                        v_decay(b, 2, par)
                    if on(b, 3):
                        dve.wait_ge(gexp, b - 3 + 1)
                        dve.reciprocal(gsum[:, :], gsum[:, :]).then_inc(ginv, 1)
                    if on(b, 2):
                        dve.wait_ge(projected, b - 2 + 1)
                        dve.wait_ge(ld_x, 16 * B // LOAD)
                        dve.tensor_tensor(res1[:, :], m0a, at(xall, b - 2), ALU.add).then_inc(res1_ready, 1)
                    if on(b, 3):
                        dve.wait_ge(ginv, b - 3 + 1)
                        before(dve, o_done, b - 3)
                        dve.tensor_scalar(gA[:, :], gex[:, :], gsum[:, 0:1], None, ALU.mult).then_inc(gA_ready, 1)
                    if on(b, 2):
                        dve.wait_ge(res1_ready, b - 2 + 1)
                        dve.bn_stats(st1[:, :], res1[:, :]).then_inc(stat1, 1)
                    if on(b, 0):
                        v_decay(b, 3, par)
                    if on(b, 2):
                        hold(dve, stat1, b - 2 + 1)
                        dve.bn_aggr(mv1[:, :], st1[:, :]).then_inc(mean1, 1)
                    if on(b, 0):
                        v_max(b, 1, par)
                    if on(b, 2):
                        dve.wait_ge(rstd1, b - 2 + 1)
                        dve.tensor_scalar(x1[:, par, :], res1[:, :], mv1[:, 0:1], rs1[:, 0:1],
                                          ALU.subtract, ALU.mult).then_inc(x1_ready, 1)
                steps(dve, step)

        iota_e = sb("iota_e", [P, E])
        thr = sb("thr", [P, MAXT])
        tile_no = sb("tile_no", [1, TILES])
        iota_i = sb("iota_i", [P, TILES + MAXT + E], I32)
        earlier = sb("earlier", [P, P])
        ones = sb("ones", [P, P])
        top1 = sb("top1", [P, B]); top2 = sb("top2", [P, B])
        oh1 = sb("oh1", [P, B, E]); oh2 = sb("oh2", [P, B, E]); both = sb("both", [P, B, E])
        work = sb("work", [P, B, E])
        idx1 = sb("idx1", [P, B]); idx2 = sb("idx2", [P, B])
        gate1 = sb("gate1", [P, B]); gate2 = sb("gate2", [P, B])
        total = sb("total", [P, B, E]); upto = sb("upto", [P, B, E]); rank = sb("rank", [P, B, E])
        need = sb("need", [P, E, MAXT]); ntiles = sb("ntiles", [P, E]); tile_end = sb("tile_end", [P, E])
        base = sb("base", [P, E])
        pos_f = sb("pos_f", [P, 2, B])
        pos = sb("pos", [P, 2, B], U32)
        begun = sb("begun", [1, TILES, E])
        texp_f = sb("texp_f", [1, TILES]); texp = sb("texp", [1, TILES], I32)
        rt_c = sem("rt_c"); rt = sem("rt"); rt_gap = sem("rt_gap"); rt_exp = sem("rt_exp")
        rt_both = sem("rt_both"); rt_rank = sem("rt_rank"); rt_tot = sem("rt_tot"); rt_read = sem("rt_read")
        rt_pos = sem("rt_pos"); scattered = sem("scattered")
        ps_rank, ps_total = ps_m[:, 0, 0:2, :], ps_m[:, 1, 0:2, :]

        def over_e(ap):
            return ap.unsqueeze(2).to_broadcast([P, B, E])

        def over_t(ap):
            return ap.unsqueeze(1).to_broadcast([P, B, E])

        with nc.Block() as block:

            @block.gpsimd
            def _(pool):
                pool.iota(iota_i[:, 0:E], pattern=[[1, E]], base=0, channel_multiplier=0).then_inc(rt_c, 1)
                pool.iota(iota_i[:, E:E + MAXT], pattern=[[TILE, MAXT]], base=0, channel_multiplier=0).then_inc(rt_c, 1)
                pool.iota(iota_i[:, E + MAXT:E + MAXT + TILES], pattern=[[1, TILES]], base=0, channel_multiplier=0).then_inc(rt_c, 1)
                pool.memset(ones[:, :], 1.0).then_inc(rt_c, 1)
                pool.wait_ge(rt_c, 4)
                pool.affine_select(out=earlier[:, :], in_=ones[:, :], compare_op=ALU.is_ge, fill=0.0,
                                   base=-1, pattern=[[1, P]], channel_multiplier=-1).then_inc(rt_c, 1)
                pool.wait_ge(cleared, 16 * (SLOTS // (4 * P) + (SLOTS % (4 * P) > 0)))
                pool.wait_ge(rt_pos, 1)
                pool.wait_ge(xhat_ready, B)
                for t in range(B):
                    for k in range(2):
                        pool.indirect_dma_start(xs_dram[:, :], bass.IndirectOffsetOnAxis(ap=pos[:, k, t:t + 1], axis=0),
                                                call[:, t, :], None).then_inc(scattered, 16)
                pool.wait_ge(ld_e, 16 * 5)
                pool.wait_ge(scattered, 16 * 2 * B)

            @block.scalar
            def _(act):
                act.wait_ge(rt_gap, 1)
                act.activation(gate2[:, :], gate1[:, :], ACT.Exp).then_inc(rt_exp, 1)

            @block.tensor
            def _(pe):
                pe.wait_ge(rt_c, 5)
                pe.wait_ge(rt_both, 1)
                pe.matmul(ps_rank, earlier[:, :], both[:, :, :].rearrange("p t e -> p (t e)"), start=True, stop=True).then_inc(rt_rank, 1)
                pe.matmul(ps_total, ones[:, :], both[:, :, :].rearrange("p t e -> p (t e)"), start=True, stop=True).then_inc(rt_tot, 1)

            @block.vector
            def _(dve):
                count = [0]

                def link(ins):
                    count[0] += 1
                    ins.then_inc(rt, 1)
                    dve.wait_ge(rt, count[0])

                def pick(best, onehot, idx):
                    link(dve.tensor_reduce(best[:, :], work[:, :, :], AX.X, ALU.max))
                    link(dve.tensor_tensor(onehot[:, :, :], work[:, :, :], over_e(best[:, :]), ALU.is_equal))
                    link(dve.scalar_tensor_tensor(out=onehot[:, :, :], in0=over_t(iota_e[:, :]), scalar=-float(E),
                                                  in1=onehot[:, :, :], op0=ALU.add, op1=ALU.mult))
                    link(dve.tensor_reduce(idx[:, :], onehot[:, :, :], AX.X, ALU.min))
                    link(dve.tensor_scalar(idx[:, :], idx[:, :], float(E), None, ALU.add))
                    link(dve.tensor_tensor(onehot[:, :, :], over_t(iota_e[:, :]), over_e(idx[:, :]), ALU.is_equal))

                dve.wait_ge(rt_c, 3)
                link(dve.tensor_copy(iota_e[:, :], iota_i[:, 0:E]))
                link(dve.tensor_copy(thr[:, :], iota_i[:, E:E + MAXT]))
                link(dve.tensor_copy(tile_no[:, :], iota_i[0:1, E + MAXT:E + MAXT + TILES]))
                dve.wait_ge(logits_ready, B)
                link(dve.tensor_copy(work[:, :, :], logits[:, :, :]))
                pick(top1, oh1, idx1)
                link(dve.scalar_tensor_tensor(out=work[:, :, :], in0=oh1[:, :, :], scalar=NEG, in1=logits[:, :, :],
                                              op0=ALU.mult, op1=ALU.add))
                pick(top2, oh2, idx2)
                dve.tensor_tensor(both[:, :, :], oh1[:, :, :], oh2[:, :, :], ALU.add).then_inc(rt_both, 1)
                dve.tensor_tensor(gate1[:, :], top2[:, :], top1[:, :], ALU.subtract).then_inc(rt_gap, 1)
                dve.wait_ge(rt_tot, 1)
                link(dve.tensor_copy(total[:, :, :].rearrange("p t e -> p (t e)"), ps_total.rearrange("p a b -> p (a b)")))
                for e in range(E):
                    last = dve.tensor_tensor_scan(upto[:, :, e], ones[:, 0:B], total[:, :, e], 0.0, ALU.mult, ALU.add)
                link(last)
                dve.wait_ge(rt_rank, 1)
                link(dve.tensor_tensor(rank[:, :, :].rearrange("p t e -> p (t e)"), ps_rank.rearrange("p a b -> p (a b)"),
                                       upto[:, :, :].rearrange("p t e -> p (t e)"), ALU.add))
                link(dve.tensor_tensor(rank[:, :, :], rank[:, :, :], total[:, :, :], ALU.subtract))
                link(dve.tensor_tensor(need[:, :, :], upto[:, B - 1, :].unsqueeze(2).to_broadcast([P, E, MAXT]),
                                       thr[:, :].unsqueeze(1).to_broadcast([P, E, MAXT]), ALU.is_gt))
                link(dve.tensor_reduce(ntiles[:, :], need[:, :, :], AX.X, ALU.add))
                link(dve.tensor_tensor_scan(tile_end[:, :], ones[:, 0:E], ntiles[:, :], 0.0, ALU.mult, ALU.add))
                link(dve.tensor_tensor(base[:, :], tile_end[:, :], ntiles[:, :], ALU.subtract))
                link(dve.tensor_tensor(begun[:, :, :], base[0:1, :].unsqueeze(1).to_broadcast([1, TILES, E]),
                                       tile_no[:, :].unsqueeze(2).to_broadcast([1, TILES, E]), ALU.is_le))
                link(dve.tensor_reduce(texp_f[:, :], begun[:, :, :], AX.X, ALU.add))
                link(dve.tensor_scalar(texp[:, :], texp_f[:, :], -1.0, None, ALU.add))
                link(dve.tensor_scalar(base[:, :], base[:, :], float(TILE), None, ALU.mult))
                link(dve.tensor_tensor(rank[:, :, :], rank[:, :, :], over_t(base[:, :]), ALU.add))
                for k, onehot in enumerate((oh1, oh2)):
                    link(dve.tensor_tensor(work[:, :, :], onehot[:, :, :], rank[:, :, :], ALU.mult))
                    link(dve.tensor_reduce(pos_f[:, k, :], work[:, :, :], AX.X, ALU.add))
                dve.tensor_copy(pos[:, :, :], pos_f[:, :, :]).then_inc(rt_pos, 1)
                dve.wait_ge(rt_exp, 1)
                link(dve.tensor_scalar(gate1[:, :], gate2[:, :], 1.0, None, ALU.add))
                link(dve.reciprocal(gate1[:, :], gate1[:, :]))
                link(dve.tensor_tensor(gate2[:, :], gate2[:, :], gate1[:, :], ALU.mult))

        w1t = sb("w1t", [P, 2, HID]); w2t = sb("w2t", [P, 2, HID]); wot = sb("wot", [P, 2, CH, D])
        xst = sb("xst", [P, 2, 2, D])
        prt = sb("prt", [P, 2, PRM]); bot = sb("bot", [P, 2, D])
        xg = sb("xg", [P, 2, TILE])
        x2c = sb("x2c", [P, 2, TILE]); sil = sb("sil", [P, 2, TILE]); hid = sb("hid", [P, CH, TILE])
        yt = sb("yt", [P, 2, 2, D])
        w_in = [sem("w_in0"), sem("w_in1")]; wo_in = [sem("wo_in0"), sem("wo_in1")]; s_in = [sem("s_in0"), sem("s_in1")]
        p_in = sem("p_in"); b_in = sem("b_in"); s_trans = sem("s_trans"); xg_ready = sem("xg_ready")
        up2 = sem("up2"); up1 = sem("up1"); biased = sem("biased"); clipped = sem("clipped"); silued = sem("silued")
        gated = sem("gated"); hid_ready = sem("hid_ready"); down = sem("down"); y_sum = sem("y_sum")
        y_ready = sem("y_ready"); y_out = [sem("y_out0"), sem("y_out1")]
        ps_x2 = [ps_m[:, 0], ps_m[:, 1]]
        ps_x1 = [ps_s[:, 0], ps_s[:, 1]]
        ps_y = [ps_t[:, 0, 0:TILE], ps_t[:, 1, 0:TILE]]
        ps_x = ps_a[:, 0:TILE]

        def half_bank(t):
            return t[:, 0:2, :].rearrange("p a b -> p (a b)")

        def tiles(eng, step, first, last):
            for i in range(first, 3):
                step(i, i % 2)
            with eng.Fori(0, (TILES - 5) // 2) as pair:
                step(2 * pair + 3, 1)
                step(2 * pair + 4, 0)
            for i in range(3 + (TILES - 5) // 2 * 2, last + 1):
                step(i, i % 2)

        def has(i, lag):
            return not isinstance(i, int) or 0 <= i - lag < TILES

        with nc.Block() as block:

            @block.sync
            def _(sp):
                def step(i, par):
                    if has(i, -1):
                        n = i + 1
                        q = 1 - par
                        e = sp.value_load(texp[0:1, bass.ds(n, 1)] if not isinstance(n, int) else texp[0:1, n:n + 1],
                                          min_val=0, max_val=E - 1)
                        rows = (xs_dram[TILE * n:TILE * (n + 1), :] if isinstance(n, int)
                                else xs_dram[bass.ds(TILE * n, TILE), :])
                        before(sp, s_trans, n - 1)
                        sp.dma_start(xst[:, q, :, :], rows.rearrange("(p a) d -> p a d", a=2)).then_inc(s_in[q], 16)
                        one = bass.ds(e, 1)
                        before(sp, up1, CH * (n - 1))
                        sp.dma_start(w2t[:, q, :], W2[one].rearrange("a d h -> (a d) h")).then_inc(w_in[q], 16)
                        sp.dma_start(w1t[:, q, :], W1[one].rearrange("a d h -> (a d) h")).then_inc(w_in[q], 16)
                        before(sp, down, CH * (n - 1))
                        sp.dma_start(wot[:, q, :, :], Wo[one].rearrange("a (p c) d -> (a p) c d", c=CH)).then_inc(wo_in[q], 16)
                tiles(sp, step, -1, TILES - 2)

            @block.gpsimd
            def _(pool):
                def step(i, par):
                    if has(i, -1):
                        n = i + 1
                        q = 1 - par
                        e = pool.value_load(texp[0:1, bass.ds(n, 1)] if not isinstance(n, int) else texp[0:1, n:n + 1],
                                            min_val=0, max_val=E - 1)
                        before(pool, gated, CH * (n - 1))
                        pool.tensor_copy(prt[:, q, :], params[:, bass.ds(e, 1), :].rearrange("p a n -> p (a n)")).then_inc(p_in, 1)
                    if has(i, 1):
                        pool.wait_ge(y_ready, i)
                        rows = (ys_dram[TILE * (i - 1):TILE * i, :] if isinstance(i, int)
                                else ys_dram[bass.ds(TILE * (i - 1), TILE), :])
                        pool.dma_start(rows.rearrange("(p a) d -> p a d", a=2), yt[:, 1 - par, :, :]).then_inc(y_out[1 - par], 16)
                    if has(i, -1):
                        before(pool, y_sum, n - 1)
                        pool.tensor_copy(bot[:, q, :], bo_rows[:, bass.ds(e, 1), :].rearrange("p a n -> p (a n)")).then_inc(b_in, 1)
                tiles(pool, step, -1, TILES)
                pool.wait_ge(y_out[0], 16 * ((TILES + 1) // 2))
                pool.wait_ge(y_out[1], 16 * (TILES // 2))

            @block.tensor
            def _(pe):
                def p_down(i, c, par):
                    pe.wait_ge(hid_ready, CH * i + c + 1)
                    if c == 0:
                        pe.wait_ge(wo_in[par], 8 * (i - par) + 16)
                    if c == 0:
                        before(pe, y_sum, i - 1)
                    for a in range(2):
                        mm = pe.matmul(ps_y[par][:, a * P:(a + 1) * P], hid[:, c, a * P:(a + 1) * P], wot[:, par, c, :],
                                       start=(c == 0 and a == 0), stop=(c == CH - 1), skip_group_check=True)
                    mm.then_inc(down, 1)

                def step(i, par):
                    for c in range(CH):
                        if has(i, 0):
                            if c == 0:
                                pe.wait_ge(w_in[par], 16 * (i - par) + 32)
                                pe.wait_ge(xg_ready, i + 1)
                            before(pe, biased, CH * i + c - 1)
                            pe.matmul(half_bank(ps_x2[c % 2]), w2t[:, par, :].rearrange("p (q c) -> p c q", c=CH)[:, c, :],
                                      xg[:, par, :], start=True, stop=True).then_inc(up2, 1)
                            before(pe, gated, CH * i + c - 1)
                            pe.matmul(half_bank(ps_x1[c % 2]), w1t[:, par, :].rearrange("p (q c) -> p c q", c=CH)[:, c, :],
                                      xg[:, par, :], start=True, stop=True).then_inc(up1, 1)
                        if c < CH - 1 and has(i, 1):
                            p_down(i - 1, c + 1, 1 - par)
                        if c == CH - 1 and has(i, 0):
                            p_down(i, 0, par)
                        if c == 1 and has(i, -1):
                            pe.wait_ge(s_in[1 - par], 8 * (i + 1 - (1 - par)) + 16)
                            for a in range(2):
                                mm = pe.transpose(ps_x[:, a * P:(a + 1) * P], xst[:, 1 - par, a, :], ident[:, :])
                            mm.then_inc(s_trans, 1)
                tiles(pe, step, -1, TILES)

            @block.scalar
            def _(act):
                def silu(k, i, c):
                    act.wait_ge(clipped, k + 1)
                    before(act, gated, k - 1)
                    act.activation(sil[:, c % 2, :], x2c[:, c % 2, :], ACT.Silu).then_inc(silued, 1)

                def step(i, par):
                    for c in range(CH):
                        k = CH * i + c
                        if has(i, 0):
                            if c == 0:
                                act.wait_ge(p_in, i + 1)
                            act.wait_ge(up2, k + 1)
                            before(act, silued, k - 1)
                            act.activation(x2c[:, c % 2, :], half_bank(ps_x2[c % 2]), ACT.Identity,
                                           bias=prt[:, par, 2 + CH + c:3 + CH + c]).then_inc(biased, 1)
                        if c > 0 and has(i, 0):
                            silu(k - 1, i, c - 1)
                        if c == 0 and has(i, 1):
                            silu(k - 1, i - 1, CH - 1)
                tiles(act, step, 0, TILES)

            @block.vector
            def _(dve):
                def gate(i, c, k, par):
                    dve.wait_ge(up1, k + 1)
                    dve.wait_ge(silued, k + 1)
                    before(dve, down, k - CH + 1)
                    dve.scalar_tensor_tensor(out=hid[:, c, :], in0=half_bank(ps_x1[c % 2]), scalar=prt[:, par, 2 + c:3 + c],
                                             in1=sil[:, c % 2, :], op0=ALU.add, op1=ALU.mult).then_inc(gated, 1)

                def hclip(c, k):
                    dve.wait_ge(gated, k + 1)
                    dve.tensor_scalar(hid[:, c, :], hid[:, c, :], 1e4, -1e4, ALU.min, ALU.max).then_inc(hid_ready, 1)

                def step(i, par):
                    for c in range(CH):
                        k = CH * i + c
                        if has(i, 0):
                            dve.wait_ge(biased, k + 1)
                            dve.tensor_scalar(x2c[:, c % 2, :], x2c[:, c % 2, :], 20.0, -20.0,
                                              ALU.min, ALU.max).then_inc(clipped, 1)
                        if c > 0 and has(i, 0):
                            gate(i, c - 1, k - 1, par)
                            hclip(c - 1, k - 1)
                        if c == 0 and has(i, 1):
                            gate(i - 1, CH - 1, k - 1, 1 - par)
                            hclip(CH - 1, k - 1)
                        if c == 2 and has(i, -1):
                            dve.wait_ge(s_trans, i + 2)
                            dve.wait_ge(p_in, i + 2)
                            dve.tensor_scalar(xg[:, 1 - par, :], ps_x, prt[:, 1 - par, 0:1], prt[:, 1 - par, 1:2],
                                              ALU.mult, ALU.add).then_inc(xg_ready, 1)
                        if c == 3 and has(i, 1):
                            dve.wait_ge(down, CH * i)
                            dve.wait_ge(b_in, i)
                            before(dve, y_out[1 - par], 8 * (i - 4 + par) + 16 if not isinstance(i, int) or i >= 3 else 0)
                            dve.tensor_tensor(yt[:, 1 - par, :, :], ps_y[1 - par].rearrange("p (a d) -> p a d", a=2),
                                              bot[:, 1 - par, :].unsqueeze(1).to_broadcast([P, 2, D]), ALU.add).then_inc(y_sum, 1)
                            dve.wait_ge(y_sum, i)
                            dve.tensor_scalar(yt[:, 1 - par, :, :], yt[:, 1 - par, :, :], 1e4, -1e4,
                                              ALU.min, ALU.max).then_inc(y_ready, 1)
                tiles(dve, step, -1, TILES)

        R = 4
        g1t = sb("g1t", [P, R, D]); g2t = sb("g2t", [P, R, D]); fin = sb("fin", [P, R, D])
        st5 = sb("st5", [P, R, 6]); mv5 = sb("mv5", [P, R, 2]); rs5 = sb("rs5", [P, R])
        got = [sem(f"got{i}") for i in range(R)]; mix1 = sem("mix1"); mix2 = sem("mix2"); stat5 = sem("stat5")
        mean5 = sem("mean5"); rstd5 = sem("rstd5"); fin_ready = sem("fin_ready"); stored = [sem(f"stored{i}") for i in range(R)]
        with nc.Block() as block:

            @block.gpsimd
            def _(pool):
                for t in range(B + 1):
                    if t < B:
                        r = t % R
                        if t >= R:
                            pool.wait_ge(mix2, t - R + 1)
                        for k, buf in enumerate((g1t, g2t)):
                            pool.indirect_dma_start(buf[:, r, :], None, ys_dram[:, :],
                                                    bass.IndirectOffsetOnAxis(ap=pos[:, k, t:t + 1], axis=0)).then_inc(got[r], 16)
                    if t >= 1:
                        u = t - 1
                        pool.wait_ge(mean5, u + 1)
                        rs = rs5[:, u % R:u % R + 1]
                        pool.tensor_tensor(rs, mv5[:, u % R, 1:2], eps_col[:, 0:1], ALU.add).then_inc(eps5, 1)
                        pool.wait_ge(eps5, u + 1)
                        pool.tensor_tensor(rs, rs, mhalf[:, 0:1], ALU.pow).then_inc(rstd5, 1)

            @block.vector
            def _(dve):
                for t in range(B + 2):
                    if t < B:
                        r = t % R
                        dve.wait_ge(got[r], 32 * (t // R + 1))
                        if t >= R:
                            dve.wait_ge(stored[r], 16 * (t // R))
                        dve.scalar_tensor_tensor(out=fin[:, r, :], in0=g1t[:, r, :], scalar=gate1[:, t:t + 1],
                                                 in1=xall[:, t, :], op0=ALU.mult, op1=ALU.add).then_inc(mix1, 1)
                        dve.wait_ge(mix1, t + 1)
                        dve.scalar_tensor_tensor(out=fin[:, r, :], in0=g2t[:, r, :], scalar=gate2[:, t:t + 1],
                                                 in1=fin[:, r, :], op0=ALU.mult, op1=ALU.add).then_inc(mix2, 1)
                        dve.wait_ge(mix2, t + 1)
                        dve.bn_stats(st5[:, r, :], fin[:, r, :]).then_inc(stat5, 1)
                        dve.wait_ge(stat5, t + 1)
                        dve.bn_aggr(mv5[:, r, :], st5[:, r, :]).then_inc(mean5, 1)
                    if t >= 2:
                        u = t - 2
                        q = u % R
                        dve.wait_ge(rstd5, u + 1)
                        dve.tensor_scalar(fin[:, q, :], fin[:, q, :], mv5[:, q, 0:1], rs5[:, q:q + 1],
                                          ALU.subtract, ALU.mult).then_inc(fin_ready, 1)

            @block.sync
            def _(sp):
                for t in range(B):
                    sp.wait_ge(fin_ready, t + 1)
                    sp.dma_start(out[t], fin[:, t % R, :]).then_inc(stored[t % R], 16)
                for r in range(R):
                    sp.wait_ge(stored[r], 16 * (B // R))


_INS = ['x', 'ctx_1024', 'L0_attn_W_q', 'L0_attn_W_k', 'L0_attn_W_v', 'L0_attn_W_o', 'L0_attn_W_down_kv',
        'L0_attn_W_up_k', 'L0_attn_W_up_v', 'L0_xattn_Wv', 'L0_xattn_bv', 'L0_xattn_Wo', 'L0_xattn_bo',
        'L0_ffn_ln_g', 'L0_ffn_ln_b', 'L0_ffn_router_w', 'L0_ffn_eg', 'L0_ffn_eb', 'L0_ffn_W1', 'L0_ffn_b1',
        'L0_ffn_W2', 'L0_ffn_b2', 'L0_ffn_Wo', 'L0_ffn_bo']
_OUTS = [((32, 128, 128), 'float32')]


def kernel(**inputs):
    import numpy as _np
    import concourse.bacc as _bacc
    from concourse import mybir as _mybir
    from concourse.bass_utils import run_bass_kernel_spmd as _run

    nc = _bacc.Bacc("TRN2", target_bir_lowering=False, num_devices=1)
    arrays, args = {}, []
    for name in _INS:
        a = _np.ascontiguousarray(inputs[name])
        arrays[f"in_{name}_dram"] = a
        args.append(nc.dram_tensor(f"in_{name}_dram", a.shape, _mybir.dt.from_np(a.dtype), kind="ExternalInput").ap())
    for i, (shape, dtype) in enumerate(_OUTS):
        dt = _mybir.dt.from_np(_np.dtype(dtype))
        args.append(nc.dram_tensor(f"out_{i}_dram", shape, dt, kind="ExternalOutput").ap())
    decoder_layer(nc, *args)
    r = _run(nc, [arrays], core_ids=[0])
    got = tuple(r.results[0][f"out_{i}_dram"] for i in range(len(_OUTS)))
    return got[0]
```
